# Optimizing a Trainium2 kernel written in Bass

```python
import numpy as np
import jax
import jax.numpy as jnp

def _softmax(x, axis=-1):
    return jax.nn.softmax(x, axis=axis)

def _gelu(x):
    return jax.nn.gelu(x, approximate=True)

def _silu(x):
    return jax.nn.silu(x)

def _sigmoid(x):
    return jax.nn.sigmoid(x)

def _layernorm(x, axis=-1, eps=1e-05):
    m = jnp.mean(x, axis=axis, keepdims=True)
    v = jnp.var(x, axis=axis, keepdims=True)
    return (x - m) / jnp.sqrt(v + eps)

def _scatter_add(tgt, idx, src, axis=0):
    return tgt.at[idx].add(src)

def _segment_sum(src, seg, n):
    return jax.ops.segment_sum(src, seg, n)
kernel_name = 'mk_adaln_d1_jaxref_r8_2eaa31'

def setup_inputs(seed: int=0):
    np.random.seed(seed)
    _w = jnp.asarray

    def _L0_attn_setup():
        import jax, jax.numpy as jnp
        import numpy as np
        B, L, FUSED, DIM = (4, 72, 256, 256)
        DI, DS, DCONV, DTR = (2 * DIM, 16, 4, 128)

        def _mamba_params(key, prefix):
            ks = jax.random.split(key, 6)
            s_in = 1.0 / np.sqrt(DIM)
            s_di = 1.0 / np.sqrt(DI)
            s_dt = 1.0 / np.sqrt(DTR)
            A_log = jnp.log(jnp.broadcast_to(jnp.arange(1, DS + 1, dtype=jnp.float32), (DI, DS)))
            return {prefix + '_in_w': jax.random.normal(ks[0], (2 * DI, DIM), jnp.float32) * s_in, prefix + '_conv_w': jax.random.normal(ks[1], (DI, DCONV), jnp.float32) * 0.5, prefix + '_conv_b': jnp.zeros((DI,), jnp.float32), prefix + '_xproj_w': jax.random.normal(ks[2], (DTR + 2 * DS, DI), jnp.float32) * s_di, prefix + '_dt_w': jax.random.normal(ks[3], (DI, DTR), jnp.float32) * s_dt, prefix + '_dt_b': jax.random.normal(ks[4], (DI,), jnp.float32) * 0.1 - 4.0, prefix + '_A_log': A_log, prefix + '_D': jnp.ones((DI,), jnp.float32), prefix + '_out_w': jax.random.normal(ks[5], (DIM, DI), jnp.float32) * s_di}

        def _dw_conv(x, w, b):
            xt = jnp.transpose(x, (0, 2, 1))
            xp = jnp.pad(xt, ((0, 0), (0, 0), (DCONV - 1, 0)))
            Ln = xt.shape[-1]
            y = b[None, :, None]
            for kk in range(DCONV):
                y = y + w[:, kk][None, :, None] * xp[:, :, kk:kk + Ln]
            return jnp.transpose(y, (0, 2, 1))

        def _selective_scan(xi, dt, Bm, Cm, A, D):

            def step(h, inp):
                dt_t, B_t, C_t, x_t = inp
                dA = jnp.exp(dt_t[..., None] * A)
                h = dA * h + (dt_t * x_t)[..., None] * B_t[:, None, :]
                y = jnp.einsum('bds,bs->bd', h, C_t)
                return (h, y)
            h0 = jnp.zeros((xi.shape[0], DI, DS), xi.dtype)
            inps = (jnp.swapaxes(dt, 0, 1), jnp.swapaxes(Bm, 0, 1), jnp.swapaxes(Cm, 0, 1), jnp.swapaxes(xi, 0, 1))
            _, ys = jax.lax.scan(step, h0, inps)
            return jnp.swapaxes(ys, 0, 1) + xi * D

        def _mamba(x, in_w, conv_w, conv_b, xproj_w, dt_w, dt_b, A_log, D, out_w):
            xz = jnp.einsum('bld,ed->ble', x, in_w)
            xi, z = jnp.split(xz, 2, axis=-1)
            xi = jax.nn.silu(_dw_conv(xi, conv_w, conv_b))
            xdb = jnp.einsum('bld,ed->ble', xi, xproj_w)
            dtr, Bm, Cm = (xdb[..., :DTR], xdb[..., DTR:DTR + DS], xdb[..., DTR + DS:])
            dt = jax.nn.softplus(jnp.einsum('blr,dr->bld', dtr, dt_w) + dt_b)
            y = _selective_scan(xi, dt, Bm, Cm, -jnp.exp(A_log), D)
            y = y * jax.nn.silu(z)
            return jnp.einsum('bld,ed->ble', y, out_w)

        def _layernorm(x, g, b, eps=1e-05):
            mu = jnp.mean(x, -1, keepdims=True)
            var = jnp.mean(jnp.square(x - mu), -1, keepdims=True)
            return (x - mu) * jax.lax.rsqrt(var + eps) * g + b
        key = jax.random.key(seed)
        k = jax.random.split(key, 8)
        inp = {'img_patches': jax.random.normal(k[0], (B, L, FUSED), jnp.float32), 'w_in': jax.random.normal(k[1], (DIM, FUSED), jnp.float32) / np.sqrt(FUSED), 'b_in': jnp.zeros((DIM,), jnp.float32), 'ln_g': jnp.ones((DIM,), jnp.float32), 'ln_b': jnp.zeros((DIM,), jnp.float32), 'w_out': jax.random.normal(k[2], (DIM, DIM), jnp.float32) / np.sqrt(DIM), 'b_out': jnp.zeros((DIM,), jnp.float32)}
        inp.update(_mamba_params(k[3], 'fm'))
        inp.update(_mamba_params(k[4], 'bm'))
        return inp
    _L0_attn_in = _L0_attn_setup()

    def _L0_ffn_setup():
        import jax, jax.numpy as jnp
        import numpy as np
        TOP_K = 2
        key = jax.random.key(seed)
        ks = jax.random.split(key, 7)
        B, S, H = (2, 256, 256)
        E, A, NS = (8, 64, 2048)
        x = jax.random.normal(ks[0], (B, S, H), jnp.float32)
        gate_w = jax.random.normal(ks[1], (E, H), jnp.float32) * 0.01
        W = jax.random.normal(ks[2], (H, H), jnp.float32) * 0.02
        atoms = jax.random.normal(ks[3], (A, NS), jnp.float32) * 0.02
        expert_atom_weights = jax.random.normal(ks[4], (E, A), jnp.float32) * 0.1
        importance = jax.random.normal(ks[5], (E, NS), jnp.float32) * 0.1
        mask_idx = jax.random.randint(ks[6], (NS,), 0, H * H, jnp.int32)
        return dict(x=x, gate_w=gate_w, W=W, atoms=atoms, expert_atom_weights=expert_atom_weights, importance=importance, mask_idx=mask_idx)
    _L0_ffn_in = _L0_ffn_setup()
    _L0_c = _w((lambda *s: np.random.randn(*s).astype(np.float32) * 0.05)(16, 256))
    _L0_wmod = _w((lambda *s: np.random.randn(*s).astype(np.float32) * 0.05)(256, 6 * 256) * 256 ** (-0.5))
    _d = {'L0_attn_img_patches': _L0_attn_in['img_patches'], 'L0_attn_w_in': _L0_attn_in['w_in'], 'L0_attn_b_in': _L0_attn_in['b_in'], 'L0_attn_fm_in_w': _L0_attn_in['fm_in_w'], 'L0_attn_fm_conv_w': _L0_attn_in['fm_conv_w'], 'L0_attn_fm_conv_b': _L0_attn_in['fm_conv_b'], 'L0_attn_fm_xproj_w': _L0_attn_in['fm_xproj_w'], 'L0_attn_fm_dt_w': _L0_attn_in['fm_dt_w'], 'L0_attn_fm_dt_b': _L0_attn_in['fm_dt_b'], 'L0_attn_fm_A_log': _L0_attn_in['fm_A_log'], 'L0_attn_fm_D': _L0_attn_in['fm_D'], 'L0_attn_fm_out_w': _L0_attn_in['fm_out_w'], 'L0_attn_bm_in_w': _L0_attn_in['bm_in_w'], 'L0_attn_bm_conv_w': _L0_attn_in['bm_conv_w'], 'L0_attn_bm_conv_b': _L0_attn_in['bm_conv_b'], 'L0_attn_bm_xproj_w': _L0_attn_in['bm_xproj_w'], 'L0_attn_bm_dt_w': _L0_attn_in['bm_dt_w'], 'L0_attn_bm_dt_b': _L0_attn_in['bm_dt_b'], 'L0_attn_bm_A_log': _L0_attn_in['bm_A_log'], 'L0_attn_bm_D': _L0_attn_in['bm_D'], 'L0_attn_bm_out_w': _L0_attn_in['bm_out_w'], 'L0_attn_ln_g': _L0_attn_in['ln_g'], 'L0_attn_ln_b': _L0_attn_in['ln_b'], 'L0_attn_w_out': _L0_attn_in['w_out'], 'L0_attn_b_out': _L0_attn_in['b_out'], 'L0_ffn_gate_w': _L0_ffn_in['gate_w'], 'L0_ffn_W': _L0_ffn_in['W'], 'L0_ffn_atoms': _L0_ffn_in['atoms'], 'L0_ffn_expert_atom_weights': _L0_ffn_in['expert_atom_weights'], 'L0_ffn_importance': _L0_ffn_in['importance'], 'L0_ffn_mask_idx': _L0_ffn_in['mask_idx'], 'L0_c': _L0_c, 'L0_wmod': _L0_wmod}
    _x0 = _d['L0_attn_img_patches']
    _d['L0_attn_img_patches'] = jax.random.normal(jax.random.fold_in(jax.random.key(seed), 1), (16, 256, 256), dtype=_x0.dtype)
    del _x0
    return _d

def reference(L0_attn_img_patches, L0_attn_w_in, L0_attn_b_in, L0_attn_fm_in_w, L0_attn_fm_conv_w, L0_attn_fm_conv_b, L0_attn_fm_xproj_w, L0_attn_fm_dt_w, L0_attn_fm_dt_b, L0_attn_fm_A_log, L0_attn_fm_D, L0_attn_fm_out_w, L0_attn_bm_in_w, L0_attn_bm_conv_w, L0_attn_bm_conv_b, L0_attn_bm_xproj_w, L0_attn_bm_dt_w, L0_attn_bm_dt_b, L0_attn_bm_A_log, L0_attn_bm_D, L0_attn_bm_out_w, L0_attn_ln_g, L0_attn_ln_b, L0_attn_w_out, L0_attn_b_out, L0_ffn_gate_w, L0_ffn_W, L0_ffn_atoms, L0_ffn_expert_atom_weights, L0_ffn_importance, L0_ffn_mask_idx, L0_c, L0_wmod):

    def _L0_attn_ref(img_patches, w_in, b_in, fm_in_w, fm_conv_w, fm_conv_b, fm_xproj_w, fm_dt_w, fm_dt_b, fm_A_log, fm_D, fm_out_w, bm_in_w, bm_conv_w, bm_conv_b, bm_xproj_w, bm_dt_w, bm_dt_b, bm_A_log, bm_D, bm_out_w, ln_g, ln_b, w_out, b_out):
        import jax, jax.numpy as jnp
        import numpy as np
        B, L, FUSED, DIM = (4, 72, 256, 256)
        DI, DS, DCONV, DTR = (2 * DIM, 16, 4, 128)

        def _mamba_params(key, prefix):
            ks = jax.random.split(key, 6)
            s_in = 1.0 / np.sqrt(DIM)
            s_di = 1.0 / np.sqrt(DI)
            s_dt = 1.0 / np.sqrt(DTR)
            A_log = jnp.log(jnp.broadcast_to(jnp.arange(1, DS + 1, dtype=jnp.float32), (DI, DS)))
            return {prefix + '_in_w': jax.random.normal(ks[0], (2 * DI, DIM), jnp.float32) * s_in, prefix + '_conv_w': jax.random.normal(ks[1], (DI, DCONV), jnp.float32) * 0.5, prefix + '_conv_b': jnp.zeros((DI,), jnp.float32), prefix + '_xproj_w': jax.random.normal(ks[2], (DTR + 2 * DS, DI), jnp.float32) * s_di, prefix + '_dt_w': jax.random.normal(ks[3], (DI, DTR), jnp.float32) * s_dt, prefix + '_dt_b': jax.random.normal(ks[4], (DI,), jnp.float32) * 0.1 - 4.0, prefix + '_A_log': A_log, prefix + '_D': jnp.ones((DI,), jnp.float32), prefix + '_out_w': jax.random.normal(ks[5], (DIM, DI), jnp.float32) * s_di}

        def _dw_conv(x, w, b):
            xt = jnp.transpose(x, (0, 2, 1))
            xp = jnp.pad(xt, ((0, 0), (0, 0), (DCONV - 1, 0)))
            Ln = xt.shape[-1]
            y = b[None, :, None]
            for kk in range(DCONV):
                y = y + w[:, kk][None, :, None] * xp[:, :, kk:kk + Ln]
            return jnp.transpose(y, (0, 2, 1))

        def _selective_scan(xi, dt, Bm, Cm, A, D):

            def step(h, inp):
                dt_t, B_t, C_t, x_t = inp
                dA = jnp.exp(dt_t[..., None] * A)
                h = dA * h + (dt_t * x_t)[..., None] * B_t[:, None, :]
                y = jnp.einsum('bds,bs->bd', h, C_t)
                return (h, y)
            h0 = jnp.zeros((xi.shape[0], DI, DS), xi.dtype)
            inps = (jnp.swapaxes(dt, 0, 1), jnp.swapaxes(Bm, 0, 1), jnp.swapaxes(Cm, 0, 1), jnp.swapaxes(xi, 0, 1))
            _, ys = jax.lax.scan(step, h0, inps)
            return jnp.swapaxes(ys, 0, 1) + xi * D

        def _mamba(x, in_w, conv_w, conv_b, xproj_w, dt_w, dt_b, A_log, D, out_w):
            xz = jnp.einsum('bld,ed->ble', x, in_w)
            xi, z = jnp.split(xz, 2, axis=-1)
            xi = jax.nn.silu(_dw_conv(xi, conv_w, conv_b))
            xdb = jnp.einsum('bld,ed->ble', xi, xproj_w)
            dtr, Bm, Cm = (xdb[..., :DTR], xdb[..., DTR:DTR + DS], xdb[..., DTR + DS:])
            dt = jax.nn.softplus(jnp.einsum('blr,dr->bld', dtr, dt_w) + dt_b)
            y = _selective_scan(xi, dt, Bm, Cm, -jnp.exp(A_log), D)
            y = y * jax.nn.silu(z)
            return jnp.einsum('bld,ed->ble', y, out_w)

        def _layernorm(x, g, b, eps=1e-05):
            mu = jnp.mean(x, -1, keepdims=True)
            var = jnp.mean(jnp.square(x - mu), -1, keepdims=True)
            return (x - mu) * jax.lax.rsqrt(var + eps) * g + b
        h = jax.nn.gelu(jnp.einsum('blf,df->bld', img_patches, w_in) + b_in, approximate=False)
        fwd = _mamba(h, fm_in_w, fm_conv_w, fm_conv_b, fm_xproj_w, fm_dt_w, fm_dt_b, fm_A_log, fm_D, fm_out_w)
        bwd = _mamba(jnp.flip(h, 1), bm_in_w, bm_conv_w, bm_conv_b, bm_xproj_w, bm_dt_w, bm_dt_b, bm_A_log, bm_D, bm_out_w)
        r = fwd + jnp.flip(bwd, 1) + h
        r = _layernorm(r, ln_g, ln_b)
        return jnp.einsum('bld,ed->ble', r, w_out) + b_out

    def _L0_ffn_ref(x, gate_w, W, atoms, expert_atom_weights, importance, mask_idx):
        import jax, jax.numpy as jnp
        import numpy as np
        TOP_K = 2
        B, S, H = x.shape
        xt = x.reshape(-1, H)
        logits = jnp.clip(xt @ gate_w.T, -50.0, 50.0)
        top_w, top_idx = jax.lax.top_k(logits, TOP_K)
        rw = jax.nn.softmax(top_w, axis=-1)
        deltas = jax.nn.softmax(expert_atom_weights, axis=-1) @ atoms
        weighted = deltas * jax.nn.sigmoid(importance)
        rows = mask_idx // H
        cols = mask_idx % H
        vals = jnp.einsum('tk,tks->ts', rw, weighted[top_idx])
        xg = xt[:, cols]
        contrib = jax.ops.segment_sum((xg * vals).T, rows, num_segments=H)
        out = xt @ W.T + contrib.T
        return out.reshape(B, S, H)
    x = L0_attn_img_patches
    mod = (_silu(L0_c) @ L0_wmod).reshape(L0_c.shape[0], 6, 1, -1)
    sa, ca, ga, sb, cb, gb = (mod[:, 0], mod[:, 1], mod[:, 2], mod[:, 3], mod[:, 4], mod[:, 5])
    ga = (2 * (ga >= 0) - 1) * jnp.maximum(jnp.abs(ga), 0.25)
    gb = (2 * (gb >= 0) - 1) * jnp.maximum(jnp.abs(gb), 0.25)
    h = _layernorm(x, axis=-1) * (1 + ca) + sa
    x = x + ga * _L0_attn_ref(h, L0_attn_w_in, L0_attn_b_in, L0_attn_fm_in_w, L0_attn_fm_conv_w, L0_attn_fm_conv_b, L0_attn_fm_xproj_w, L0_attn_fm_dt_w, L0_attn_fm_dt_b, L0_attn_fm_A_log, L0_attn_fm_D, L0_attn_fm_out_w, L0_attn_bm_in_w, L0_attn_bm_conv_w, L0_attn_bm_conv_b, L0_attn_bm_xproj_w, L0_attn_bm_dt_w, L0_attn_bm_dt_b, L0_attn_bm_A_log, L0_attn_bm_D, L0_attn_bm_out_w, L0_attn_ln_g, L0_attn_ln_b, L0_attn_w_out, L0_attn_b_out)
    h = _layernorm(x, axis=-1) * (1 + cb) + sb
    x = x + gb * _L0_ffn_ref(h, L0_ffn_gate_w, L0_ffn_W, L0_ffn_atoms, L0_ffn_expert_atom_weights, L0_ffn_importance, L0_ffn_mask_idx)
    return x

_drawn_inputs = setup_inputs


def setup_inputs(seed=0):
    import zlib

    import numpy as np

    out = dict(_drawn_inputs(seed))
    spreads = {'L0_attn_b_in': (0.0, 0.1),
     'L0_attn_fm_conv_b': (0.0, 0.8),
     'L0_attn_fm_D': (1.0, 0.6),
     'L0_attn_bm_conv_b': (0.0, 0.8),
     'L0_attn_bm_D': (1.0, 0.6),
     'L0_attn_ln_g': (1.0, 0.2),
     'L0_attn_ln_b': (0.0, 0.332),
     'L0_attn_b_out': (0.0, 0.35)}
    factors = {'L0_attn_fm_xproj_w': 8.0,
     'L0_attn_fm_dt_w': 8.0,
     'L0_attn_fm_dt_b': 38.379,
     'L0_attn_fm_A_log': 8.0,
     'L0_attn_bm_xproj_w': 8.0,
     'L0_attn_bm_dt_w': 8.0,
     'L0_attn_bm_dt_b': 30.262,
     'L0_attn_bm_A_log': 8.0,
     'L0_ffn_gate_w': 64.0,
     'L0_ffn_atoms': 50.777,
     'L0_ffn_expert_atom_weights': 64.0,
     'L0_ffn_importance': 64.0}
    for name, (base, spread) in spreads.items():
        noise = np.random.default_rng([zlib.crc32(name.encode()), seed]).standard_normal(out[name].shape)
        drawn = base * np.exp(spread * noise) if base else spread * noise
        out[name] = jnp.asarray(drawn.astype(out[name].dtype))
    for name, factor in factors.items():
        out[name] = (out[name] * factor).astype(out[name].dtype)
    return out
```

```python
from contextlib import ExitStack

import concourse.bass as bass
from concourse import mybir

F32 = mybir.dt.float32
BF16 = mybir.dt.bfloat16
I32 = mybir.dt.int32
ALU = mybir.AluOpType
ACT = mybir.ActivationFunctionType
AX_X = mybir.AxisListType.X

P = 128
N_SEQ, T, D = 16, 256, 256
DI, DS, TAPS, DTR = 512, 16, 4, 128
FB = D // P
JB = DI // P
TT = T // P
SQ = 4
NQ = DS // SQ
STEPS = NQ * JB
DECAY_BUFS = 4
STATE_BUFS = 8
PE_AT = dict(z=0, z2=0, x_proj=3, dt=5, dt2=6, x=10, x2=10, turn_x=7, w_in=9, join=2, turn_r=9, attention=10,
             turn_r2=0, logits=2, ffn=3, sum_lag=1, spread_ahead=7)
ACT_AT = dict(xi=3, z=3, x_proj=6, dt=8, dt2=9, exp_ln=9, x=13, x2=13, norm_x=6, modulate=10, keep=9, gelu=11,
              norm_r=10, affine=12, norm_r2=1, affine2=3, gap=6, copy_ahead=4)
DVE_AT = dict(split=6, rounded=8, log1p=11, conv=12, stats_x=2, stats_r=6, residual=12, gates=3, gates2=4,
              weigh=4, y=1)
POOL_AT = dict(rounding=11, softplus=14, diagonals=12, factors_x=4, factors_r=8, factors_r2=15, pairs_lag=3)
SUM_LAG, SPREAD_AHEAD = PE_AT["sum_lag"], PE_AT["spread_ahead"]
COPY_AHEAD = ACT_AT["copy_ahead"]
PAIRS_LAG = POOL_AT["pairs_lag"]
E, A, NS = 8, 64, 2048
NCH = NS // P
EPS = 1e-5
SP = 5
LN_MARGIN = 2.0 ** -29
FWD, BWD = 0, 1
SMALL = 32 * 3
CW, CB, DB, DD, AL, PER_DIR = 0, 16, 20, 24, 28, 28 + JB * DS
BI = 2 * PER_DIR
LG, LB, GW = BI + FB, BI + 2 * FB, BI + 3 * FB
N_SMALL = GW + FB * E
PAIRED = (1, 2, 3, 5, 6, 7, 9, 10, 11)
EARLY = (4, 4, 2, 4, 2, 8, 2)
N_EARLY = sum(EARLY)


def early(group):
    return range(sum(EARLY[:group]), sum(EARLY[:group + 1]))


def chunks_at(slot):
    rest = E * NCH - N_EARLY
    return range(N_EARLY + rest * slot // (2 * STEPS), N_EARLY + rest * (slot + 1) // (2 * STEPS))


SA, CA, GA, SB_, CB_, GB = range(6)


def build(nc, x, smalls, w_in, in_w, xproj, dt_w, out_w, w_out, w_ffn, b_out, eaw, atoms, imp, idx, c_in, wmod, out):
    rows_dram = nc.dram_tensor("mod_rows_scratch", [N_SEQ, 2, D], F32).ap()
    cols_dram = nc.dram_tensor("mod_cols_scratch", [N_SEQ, P, 12], F32).ap()
    x_seq = x.rearrange("b (t p) f -> b p t f", p=P)
    out_seq = out.rearrange("b (t p) f -> b p t f", p=P)

    with ExitStack() as ctx:
        def sb(name, shape, dt=F32):
            return ctx.enter_context(nc.sbuf_tensor(name, shape, dt))

        def ps(name, shape):
            return ctx.enter_context(nc.psum_tensor(name, shape, F32))

        def sem(name):
            return ctx.enter_context(nc.semaphore(name))

        y_ps = ps("y_ps", [P, JB, T])
        bc_ps = ps("bc_ps", [P, 2, 2 * T])
        a_ps = ps("a_ps", [P, 2, 2 * T])
        v_ps = ps("v_ps", [P, 2, 2 * T])

        small = sb("small", [P, N_SMALL])
        w_in_sb = sb("w_in_sb", [P, FB, D])
        in_w_sb = sb("in_w_sb", [P, 2, FB, 2 * DI])
        xproj_sb = sb("xproj_sb", [P, 2, JB, DTR + SMALL])
        dt_w_sb = sb("dt_w_sb", [P, 2, DI])
        out_w_sb = sb("out_w_sb", [P, 2, JB, D])
        w_out_sb = sb("w_out_sb", [P, FB, D])
        experts = sb("experts", [P, FB, (E + 1) * D])
        b_out_sb = sb("b_out_sb", [1, D])
        ones = sb("ones", [1, P])
        ident = sb("ident", [P, P])
        sel = sb("sel", [SMALL, 32], BF16)
        diag_d = sb("diag_d", [P, JB, P])
        neg_a = sb("neg_a", [P, 2, JB, DS])
        minus_half = sb("minus_half", [P, TT])
        iota_f = sb("iota_f", [P, D])
        rank = sb("rank", [P, TT, E])
        weighted = sb("weighted", [P, NCH, E])
        idx_i = sb("idx_i", [P, NCH], I32)
        rc_i = sb("rc_i", [P, 2, NCH], I32)
        rc_f = sb("rc_f", [P, 2, NCH])
        wmod_sb = experts[:, :, 0:6 * D]
        c_t = sb("c_t", [P, FB, N_SEQ])
        mod_cols = sb("mod_cols", [P, N_SEQ, 12])
        eaw_sb = sb("eaw_sb", [E, A])
        eaw_s = sb("eaw_s", [E, 4])
        eaw_t = sb("eaw_t", [A, E])

        x_buf = sb("x_buf", [P, TT * D])
        x_in = x_buf[:].rearrange("p (t f) -> p t f", f=D)
        x_norm = x_in
        h_t = x_buf[:].rearrange("p (f t) -> p f t", t=T)
        x_st = sb("x_st", [P, TT, 6])
        x_mv = sb("x_mv", [P, TT, 2])
        x_var = sb("x_var", [P, 2, TT])
        x_rstd = sb("x_rstd", [P, TT])
        x_off = sb("x_off", [P, TT])
        mod_p = sb("mod_p", [P, 12])
        h0_t = sb("h0_t", [P, FB, T])
        h0_keep = sb("h0_keep", [P, FB, T])
        x_pad = sb("x_pad", [P, JB, T + 2 * (TAPS - 1)])
        xi = [sb(f"xi{d}", [P, JB, T]) for d in (FWD, BWD)]
        z = [sb(f"z{d}", [P, JB, T]) for d in (FWD, BWD)]
        dt = [sb(f"dt{d}", [P, JB, T]) for d in (FWD, BWD)]
        u = [sb(f"u{d}", [P, JB, T]) for d in (FWD, BWD)]
        sp_e = sb("sp_e", [P, JB, T])
        sp_l = sb("sp_l", [P, JB, T])
        dtr_t = sb("dtr_t", [P, T])
        bc_raw = sb("bc_raw", [SMALL, T])
        bc_rest = sb("bc_rest", [SMALL, T])
        bc_mid = sb("bc_mid", [SMALL, T], BF16)
        bc = [sb(f"bc{d}", [SMALL, T], BF16) for d in (FWD, BWD)]

        b_all = sb("b_all", [P, 2, SQ, T])
        c_all = sb("c_all", [P, 2, SQ, T])
        decay = sb("decay", [P, DECAY_BUFS, SQ, T])
        h = sb("h", [P, STATE_BUFS, SQ, T])
        late = sb("late", [P, 8, TT * D])
        y_t = [sb("y_t0", [P, JB, T]), late[:, 5:7, :].rearrange("p a (b t) -> p (a b) t", t=T)]
        mod_rows = h[0:N_SEQ, 4, 0:2, :]
        c_sb = y_t[FWD][0:N_SEQ, 0, :]
        scaled_more = sb("scaled_more", [P, 2, D])
        scaled_row = [experts[:, 0, (E - 1) * D:E * D], experts[:, 1, (E - 1) * D:E * D],
                      scaled_more[:, 0, :], scaled_more[:, 1, :]]
        atoms_sb = h[0:A, 0:2, :, :].rearrange("p a s t -> p (a s t)")

        iota_i = late[:, 0, 0:D].bitcast(I32)
        col_hot = late[:, :, :].rearrange("p a (b f) -> p (a b) f", f=D)

        def late_view(i):
            return late[:, i, :].rearrange("p (t f) -> p t f", f=D)

        x_res, gates_bc, r_norm, x1, acc = [late_view(i) for i in range(5)]
        r_t, h2_t = r_norm, r_norm
        r_st = sb("r_st", [P, TT, 6])
        r_mv = sb("r_mv", [P, TT, 2])
        r_var = sb("r_var", [P, 2, TT])
        r_rstd = sb("r_rstd", [P, TT])
        r_off = sb("r_off", [P, TT])
        mod_f = sb("mod_f", [P, 12])
        lg = sb("lg", [P, TT, E])
        lg2 = sb("lg2", [P, TT, E])
        hot = sb("hot", [P, 2, TT, E])
        top = sb("top", [P, 4, TT])
        soft = sb("soft", [P, 3, TT])
        spare = sb("spare", [P, 1])
        gate = sb("gate", [P, TT, E])

        mod_w_loaded = sem("mod_w_loaded")
        in_w_loaded = sem("in_w_loaded")
        experts_loaded = sem("experts_loaded")
        out_w_loaded = sem("out_w_loaded")
        soft_act = sem("soft_act")
        soft_dve = sem("soft_dve")
        soft_pe = sem("soft_pe")
        x_loaded = sem("x_loaded")
        mod_p_loaded = sem("mod_p_loaded")
        res_loaded = sem("res_loaded")
        stored = sem("stored")
        mod_stored = sem("mod_stored")
        consts_ready = sem("consts_ready")
        pool_init = sem("pool_init")
        dve_init = sem("dve_init")
        dve_start = sem("dve_start")
        act_init = sem("act_init")
        pe_init = sem("pe_init")
        hot_made = sem("hot_made")
        hot_used = sem("hot_used")
        expert_read = sem("expert_read")
        x_stats = sem("x_stats")
        x_factors = sem("x_factors")
        x_normed = sem("x_normed")
        kept = sem("kept")
        a_made = sem("a_made")
        a_read = sem("a_read")
        conv_step = sem("conv_step")
        xi_ready = sem("xi_ready")
        bc_split = sem("bc_split")
        sp_made = sem("sp_made")
        sp_step = sem("sp_step")
        dt_ready = sem("dt_ready")
        u_ready = sem("u_ready")
        bc_made = sem("bc_made")
        bc_copied = sem("bc_copied")
        exp_done = sem("exp_done")
        w_done = sem("w_done")
        scan_done = sem("scan_done")
        decay_reset = sem("decay_reset")
        p_done = sem("p_done")
        pairs_done = sem("pairs_done")
        sum_done = sem("sum_done")
        y_done = sem("y_done")
        r_made = sem("r_made")
        r_stats = sem("r_stats")
        r_factors = sem("r_factors")
        r_normed = sem("r_normed")
        r_turned = sem("r_turned")
        r_scaled = sem("r_scaled")
        attn_made = sem("attn_made")
        x1_step = sem("x1_step")
        lg_made = sem("lg_made")
        gate_step = sem("gate_step")
        gap_made = sem("gap_made")
        ffn_made = sem("ffn_made")
        ffn_read = sem("ffn_read")
        fin_step = sem("fin_step")
        gate_aux = sem("gate_aux")
        gate_aux2 = sem("gate_aux2")
        v_free = sem("v_free")
        acc_step = sem("acc_step")
        diag_ready = sem("diag_ready")
        neg_a_ready = sem("neg_a_ready")

        block = ctx.enter_context(nc.Block())

        def at_least(eng, s, value):
            if not isinstance(value, int) or value > 0:
                eng.wait_ge(s, value)

        def scan_order(ap, d):
            flat = ap.rearrange("p s t -> p (s t)")
            return flat if d == FWD else flat[:, ::-1]

        TURN_USE, IN_USE = 0, 1
        X_USE, Z_USE, XP_USE, DT_USE = (2, 9), (4, 11), (6, 13), (7, 14)

        def a_use(m, use):
            return 16 * m + use

        def a_bank(use):
            return a_ps[:, use % 2, :].rearrange("p (a t) -> p a t", t=T)

        def col(d, at, n=1):
            return small[:, d * PER_DIR + at:d * PER_DIR + at + n]

        MOD_W = ((c_sb, c_in), (wmod_sb, wmod))
        IN_W = ((small[:], smalls), (w_in_sb[:], w_in), (in_w_sb[:], in_w), (xproj_sb[:], xproj), (dt_w_sb[:], dt_w))
        EXPERTS_W = ((eaw_sb[:], eaw), (atoms_sb, atoms), (weighted[:], imp), (idx_i[:], idx))
        OUT_W = ((out_w_sb[:], out_w), (w_out_sb[:], w_out), (b_out_sb[:], b_out))

        @block.sync
        def _(sp):
            def load_x(m):
                at_least(sp, a_made, 16 * (m - 1) + 2)
                sp.dma_start(x_in, x_seq[bass.ds(m, 1)].rearrange("o p t f -> (o p) t f")).then_inc(x_loaded, 16)

            def load_mod(m):
                at_least(sp, a_read, 16 * (m - 1) + 1)
                sp.dma_start(mod_p[:], cols_dram[bass.ds(m, 1)].rearrange("o p c -> (o p) c")).then_inc(mod_p_loaded, 16)

            def load_finish(m):
                if isinstance(m, int) and m == 0:
                    sp.wait_ge(hot_used, NCH * E)
                else:
                    sp.wait_ge(stored, 16 * m)
                sp.dma_start(x_res, x_seq[bass.ds(m, 1)].rearrange("o p t f -> (o p) t f")).then_inc(res_loaded, 16)
                sp.dma_start(mod_f[:], cols_dram[bass.ds(m, 1)].rearrange("o p c -> (o p) c")).then_inc(res_loaded, 16)
                sp.dma_start(gates_bc, rows_dram[bass.ds(m, 1)].broadcast_to([P, 2, D])).then_inc(res_loaded, 16)

            def store(m):
                at_least(sp, fin_step, 2 * (m + 1))
                sp.dma_start(out_seq[bass.ds(m, 1)].rearrange("o p t f -> (o p) t f"), acc).then_inc(stored, 16)

            load_x(0)
            for loaded, pairs in ((mod_w_loaded, MOD_W), (experts_loaded, EXPERTS_W), (in_w_loaded, IN_W),
                                  (out_w_loaded, OUT_W)):
                for dst, src in pairs:
                    sp.dma_start(dst, src).then_inc(loaded, 16)
            sp.wait_ge(dve_init, 4)
            sp.dma_start(rows_dram.rearrange("b g f -> b (g f)"),
                         mod_rows.rearrange("b g f -> b (g f)")).then_inc(mod_stored, 16)
            sp.dma_start(cols_dram.rearrange("b p c -> p b c"), mod_cols[:]).then_inc(mod_stored, 16)
            sp.dma_start(experts[:, :, E * D:], w_ffn).then_inc(out_w_loaded, 16)
            sp.wait_ge(mod_stored, 32)
            load_mod(0)
            load_x(1)
            load_mod(1)
            load_finish(0)
            load_x(2)
            load_mod(2)
            store(0)
            with sp.Fori(2, N_SEQ - 1) as n:
                load_finish(n - 1)
                load_x(n + 1)
                load_mod(n + 1)
                store(n - 1)
            load_finish(N_SEQ - 2)
            store(N_SEQ - 2)
            load_finish(N_SEQ - 1)
            store(N_SEQ - 1)
            sp.wait_ge(stored, 16 * N_SEQ)

        @block.gpsimd
        def _(pool):
            pool.memset(ident[:], 0.0).then_inc(pool_init, 1)
            pool.memset(sel[:], 0.0).then_inc(pool_init, 1)
            pool.memset(minus_half[:], -0.5)
            pool.memset(ones[:], 1.0)
            pool.iota(iota_i, pattern=[[1, D]], base=0, channel_multiplier=0)
            pool.memset(x_pad[:, :, 0:TAPS - 1], 0.0)
            pool.memset(x_pad[:, :, TAPS - 1 + T:], 0.0)
            pool.wait_ge(pool_init, 2)
            pool.affine_select(out=ident[:], in_=ident[:], compare_op=ALU.not_equal, fill=1.0, base=0,
                               pattern=[[-1, P]], channel_multiplier=1)
            for part in range(3):
                if part:
                    pool.wait_ge(pool_init, 2 + part)
                pool.affine_select(out=sel[:], in_=sel[:], compare_op=ALU.not_equal, fill=1.0, base=-32 * part,
                                   pattern=[[-1, 32]], channel_multiplier=1).then_inc(pool_init, 1)
            pool.wait_ge(pool_init, 5)
            for e in range(E):
                last = pool.memset(rank[:, :, e:e + 1], float(E - e))
            last.then_inc(consts_ready, 1)

            def norm_factors(var, rstd, off, steps, count):
                pool.tensor_tensor(rstd[:], var[:, 0, :], minus_half[:], ALU.pow).then_inc(steps, 1)
                pool.wait_ge(steps, count + 1)
                pool.tensor_tensor(off[:], var[:, 1, :], rstd[:], ALU.mult).then_inc(steps, 1)

            def first_factors(m):
                pool.wait_ge(x_stats, 3 * (m + 1))
                at_least(pool, x_normed, m)
                norm_factors(x_var, x_rstd, x_off, x_factors, 2 * m)

            def finish_factors(m, which):
                pool.wait_ge(r_stats, 3 * (2 * m + which + 1))
                if which:
                    pool.wait_ge(r_normed, 2 * m + 1)
                norm_factors(r_var, r_rstd, r_off, r_factors, 2 * (2 * m + which))

            def softplus(m, d, part):
                un = 2 * m + d
                if part == 1:
                    pool.wait_ge(sp_step, SP * un + 1)
                    pool.tensor_tensor(u[d][:], sp_e[:], u[d][:], ALU.subtract).then_inc(sp_step, 1)
                elif part == 2:
                    pool.wait_ge(sp_step, SP * un + 5)
                    pool.tensor_tensor(dt[d][:], u[d][:], dt[d][:], ALU.add).then_inc(dt_ready, 1)
                else:
                    pool.wait_ge(dt_ready, un + 1)
                    pool.wait_ge(xi_ready, un + 1)
                    pool.tensor_tensor(u[d][:], dt[d][:], xi[d][:], ALU.mult).then_inc(u_ready, 1)

            def times_b(n, d, k):
                un, q, j = 2 * n + d, k // JB, k % JB
                s = STEPS * un + k
                if k == 0:
                    pool.wait_ge(u_ready, un + 1)
                    if isinstance(n, int) and n == 0 and d == 0:
                        pool.wait_ge(soft_pe, 2)
                        pool.wait_ge(mod_stored, 32)
                if j == 0:
                    pool.wait_ge(bc_copied, 4 * (NQ * un + q) + 2)
                at_least(pool, sum_done, s - STATE_BUFS + 1)
                pool.tensor_tensor(h[:, k % STATE_BUFS], u[d][:, j:j + 1, :].broadcast_to([P, SQ, T]), b_all[:, q % 2],
                                   ALU.mult).then_inc(w_done, 1)

            def diagonals(un, d):
                at_least(pool, sum_done, STEPS * (un - 1) + JB)
                pool.tensor_tensor(diag_d[:], ident[:, None, :].broadcast_to([P, JB, P]),
                                   col(d, DD, JB)[:, :, None].broadcast_to([P, JB, P]), ALU.mult)\
                    .then_inc(diag_ready, 1)

            def add_pairs(un, k):
                pool.wait_ge(p_done, STEPS * un + k + 1)
                pool.tensor_tensor(h[:, k % STATE_BUFS, 0:2], h[:, k % STATE_BUFS, 0:2], h[:, k % STATE_BUFS, 2:4], ALU.add)\
                    .then_inc(pairs_done, 1)

            def turn(n, more, before):
                for d in (FWD, BWD):
                    for k in range(STEPS):
                        times_b(n, d, k)
                        if k >= PAIRS_LAG and k - PAIRS_LAG in PAIRED:
                            add_pairs(2 * n + d, k - PAIRS_LAG)
                        elif k < PAIRS_LAG and k - PAIRS_LAG + STEPS in PAIRED and not (isinstance(n, int) and 2 * n + d == 0):
                            add_pairs(2 * n + d - 1, k - PAIRS_LAG + STEPS)
                        if d == FWD or more:
                            if k == POOL_AT["diagonals"]:
                                diagonals(2 * n + d + 1, 1 - d)
                            if k == POOL_AT["rounding"]:
                                softplus(n + d, 1 - d, 1)
                            if k == POOL_AT["softplus"]:
                                softplus(n + d, 1 - d, 2)
                                softplus(n + d, 1 - d, 3)
                        if d == FWD and more and k == POOL_AT["factors_x"]:
                            first_factors(n + 1)
                        if d == FWD and before and k == POOL_AT["factors_r"]:
                            finish_factors(n - 1, 0)
                        if d == FWD and before and k == POOL_AT["factors_r2"]:
                            finish_factors(n - 1, 1)

            first_factors(0)
            pool.wait_ge(in_w_loaded, 16 * len(IN_W))
            pool.wait_ge(consts_ready, 1)
            diagonals(0, FWD)
            for part in range(1, 4):
                softplus(0, FWD, part)
            turn(0, True, False)
            with pool.Fori(1, N_SEQ - 1) as n:
                turn(n, True, True)
            turn(N_SEQ - 1, False, True)
            for k in range(STEPS - PAIRS_LAG, STEPS):
                if k in PAIRED:
                    add_pairs(2 * N_SEQ - 1, k)
            finish_factors(N_SEQ - 1, 0)
            finish_factors(N_SEQ - 1, 1)

        @block.scalar
        def _(act):
            act.wait_ge(mod_w_loaded, 16 * len(MOD_W))
            act.activation(c_sb, c_sb, ACT.Silu).then_inc(act_init, 1)

            def rates():
                for d in (FWD, BWD):
                    act.activation(neg_a[:, d].rearrange("p j s -> p (j s)"), col(d, AL, JB * DS), ACT.Exp)\
                        .then_inc(act_init, 1)

            def softmax_parts():
                act.wait_ge(experts_loaded, 16 * len(EXPERTS_W))
                act.wait_ge(soft_dve, 1)
                act.activation(eaw_sb[:], eaw_sb[:], ACT.Exp, bias=eaw_s[:, 0:1],
                               accum_out=eaw_s[:, 1:2]).then_inc(soft_act, 1)
                act.activation(weighted[:], weighted[:], ACT.Exp, scale=-1.0).then_inc(soft_act, 1)

            def use_exp_ln():
                act.preload_act_table_set("natural_log_exp_and_others")

            def normalise_x(m):
                act.wait_ge(x_factors, 2 * (m + 1))
                act.wait_ge(x_loaded, 16 * (m + 1))
                for t in range(TT):
                    last = act.activation(x_norm[:, t, :], x_in[:, t, :], ACT.Identity,
                                          bias=x_off[:, t:t + 1], scale=x_rstd[:, t:t + 1])
                last.then_inc(x_normed, 1)

            def modulate(m):
                act.wait_ge(a_made, 16 * m + 1)
                act.wait_ge(mod_p_loaded, 16 * (m + 1))
                for f in range(FB):
                    last = act.activation(h_t[:, f, :], a_bank(TURN_USE)[:, f, :], ACT.Identity,
                                          bias=mod_p[:, 2 * SA + f:2 * SA + f + 1],
                                          scale=mod_p[:, 2 * CA + f:2 * CA + f + 1])
                last.then_inc(a_read, 1)

            def keep_h0(m):
                at_least(act, r_made, m)
                act.activation(h0_keep[:], h0_t[:], ACT.Copy).then_inc(kept, 1)

            def gelu(m):
                at_least(act, kept, m)
                act.wait_ge(a_made, 16 * m + 2)
                for f in range(FB):
                    last = act.activation(h0_t[:, f, :], a_bank(IN_USE)[:, f, :], ACT.Gelu,
                                          bias=small[:, BI + f:BI + f + 1])
                last.then_inc(a_read, 1)

            def copy_xi(m, d, c):
                un = 2 * m + d
                act.wait_ge(a_made, a_use(m, X_USE[d]) + c + 1)
                if c == 0:
                    at_least(act, conv_step, TAPS * un)
                act.activation(x_pad[:, 2 * c:2 * c + 2, TAPS - 1:TAPS - 1 + T], a_bank(X_USE[d] + c), ACT.Copy)\
                    .then_inc(a_read, 1)

            def silu_z(m, d, c):
                un = 2 * m + d
                act.wait_ge(a_made, a_use(m, Z_USE[d]) + c + 1)
                at_least(act, y_done, 2 * (un - 2) + c + 1)
                act.activation(z[d][:, 2 * c:2 * c + 2, :], a_bank(Z_USE[d] + c), ACT.Silu).then_inc(a_read, 1)

            def silu_xi(m, d):
                act.wait_ge(conv_step, TAPS * (2 * m + d + 1))
                act.activation(xi[d][:], xi[d][:], ACT.Silu).then_inc(xi_ready, 1)

            def copy_xproj(m, d):
                un = 2 * m + d
                bank = a_ps[:, XP_USE[d] % 2, :]
                act.wait_ge(a_made, a_use(m, XP_USE[d]) + 1)
                at_least(act, bc_split, 2 * un)
                at_least(act, bc_made, STEPS * (un - 1))
                act.activation(bc_raw[:], bank[0:SMALL, T:2 * T], ACT.Copy)
                act.activation(bc[d][:], bank[0:SMALL, T:2 * T], ACT.Copy)
                act.activation(dtr_t[:], bank[:, 0:T], ACT.Copy).then_inc(a_read, 1)

            def take_dt(m, d, c):
                un = 2 * m + d
                bank = a_bank(DT_USE[d] + c)
                act.wait_ge(a_made, a_use(m, DT_USE[d]) + c + 1)
                if c == 0:
                    at_least(act, u_ready, un - 1)
                    at_least(act, sp_step, SP * un)
                for jj in range(2):
                    j = 2 * c + jj
                    act.activation(dt[d][:, j, :], bank[:, jj, :], ACT.Relu, bias=col(d, DB + j))
                    last = act.activation(sp_e[:, j, :], bank[:, jj, :], ACT.Abs, bias=col(d, DB + j))
                last.then_inc(a_read, 1)

            def exp_ln(m, d):
                act.wait_ge(a_read, a_use(m, DT_USE[d]) + 2)
                act.activation(sp_e[:], sp_e[:], ACT.Exp, scale=-1.0).then_inc(sp_made, 1)
                act.wait_ge(sp_made, 2 * (2 * m + d) + 1)
                act.activation(sp_l[:], sp_e[:], ACT.Ln, bias=1.0).then_inc(sp_made, 1)

            def copy_bc(n, d, q, r):
                g = NQ * (2 * n + d) + q
                act.wait_ge(bc_made, 4 * g + r + 1)
                if r == 0:
                    at_least(act, w_done, JB * (g - 1))
                if r == 2:
                    at_least(act, p_done, JB * (g - 1))
                dst = (b_all if r < 2 else c_all)[:, q % 2, 2 * (r % 2):2 * (r % 2) + 2, :]
                act.activation(dst, bc_ps[:, r % 2, :].rearrange("p (a t) -> p a t", t=T), ACT.Copy)\
                    .then_inc(bc_copied, 1)

            def decays(n, d, k):
                un, q, j = 2 * n + d, k // JB, k % JB
                s = STEPS * un + k
                if k == 0:
                    act.wait_ge(dt_ready, un + 1)
                    if isinstance(n, int) and un == 0:
                        act.wait_ge(neg_a_ready, 1)
                at_least(act, scan_done, s - DECAY_BUFS + 1)
                lo, hi = (1, T) if d == FWD else (0, T - 1)
                for i in range(SQ):
                    last = act.activation(decay[:, k % DECAY_BUFS, i, lo:hi], dt[d][:, j, lo:hi], ACT.Exp,
                                          scale=neg_a[:, d, j, SQ * q + i:SQ * q + i + 1])
                last.then_inc(exp_done, 1)

            def normalise(m, which):
                act.wait_ge(r_factors, 2 * (2 * m + which + 1))
                for t in range(TT):
                    src = v_ps[:, 0, t * D:(t + 1) * D] if which == 0 else x1[:, t, :]
                    last = act.activation(r_norm[:, t, :], src, ACT.Identity,
                                          bias=r_off[:, t:t + 1], scale=r_rstd[:, t:t + 1])
                last.then_inc(r_normed, 1)

            def affine(m, which):
                act.wait_ge(r_turned, 2 * m + which + 1)
                if which:
                    act.wait_ge(res_loaded, 48 * (m + 1))
                for f in range(FB):
                    if which == 0:
                        scale, bias, dst = small[:, LG + f:LG + f + 1], small[:, LB + f:LB + f + 1], r_t
                    else:
                        scale = mod_f[:, 2 * CB_ + f:2 * CB_ + f + 1]
                        bias = mod_f[:, 2 * SB_ + f:2 * SB_ + f + 1]
                        dst = h2_t
                    last = act.activation(dst[:, f, :], v_ps[:, 1, f * T:(f + 1) * T], ACT.Identity,
                                          bias=bias, scale=scale)
                last.then_inc(r_scaled, 1)

            def gap(m):
                act.wait_ge(gate_step, 12 * m + 8)
                act.activation(soft[:, 1, :], soft[:, 0, :], ACT.Exp).then_inc(gap_made, 1)

            def copy_expert(e):
                act.wait_ge(hot_used, NCH * (e + 1))
                if e == 0:
                    act.wait_ge(mod_stored, 32)
                act.activation(experts[:, :, e * D:(e + 1) * D],
                               v_ps[:, e % 2, :].rearrange("p (f r) -> p f r", r=D), ACT.Copy)\
                    .then_inc(v_free if e == E - 1 else expert_read, 1)

            def turn(n, more, before):
                at = ACT_AT
                first_turn = isinstance(n, int) and n == 0
                for d in (FWD, BWD):
                    unit_follows = d == FWD or more
                    for k in range(STEPS):
                        if k - 1 in (at["xi"], at["z"]) and unit_follows or k - 1 == at["gelu"] and d == FWD and more:
                            use_exp_ln()
                        decays(n, d, k)
                        q, r = divmod(k + COPY_AHEAD, 4)
                        if q < NQ:
                            copy_bc(n, d, q, r)
                        elif unit_follows:
                            copy_bc(n + d, 1 - d, q - NQ, r)
                        if unit_follows:
                            m, o = n + d, 1 - d
                            if k == at["xi"]:
                                silu_xi(m, o)
                            if k == at["z"]:
                                silu_z(m, o, 0)
                                silu_z(m, o, 1)
                            if k == at["x_proj"]:
                                copy_xproj(m, o)
                            if k == at["dt"]:
                                take_dt(m, o, 0)
                            if k == at["dt2"]:
                                take_dt(m, o, 1)
                            if k == at["exp_ln"]:
                                exp_ln(m, o)
                        if more and k == at["x"]:
                            copy_xi(n + 1, d, 0)
                        if more and k == at["x2"]:
                            copy_xi(n + 1, d, 1)
                        if d == FWD:
                            if more and k == at["norm_x"]:
                                normalise_x(n + 1)
                            if more and k == at["modulate"]:
                                modulate(n + 1)
                            if k == at["keep"]:
                                keep_h0(n)
                            if more and k == at["gelu"]:
                                gelu(n + 1)
                            if before and k == at["norm_r"]:
                                normalise(n - 1, 0)
                            if before and k == at["affine"]:
                                affine(n - 1, 0)
                        elif before:
                            if k == at["norm_r2"]:
                                normalise(n - 1, 1)
                            if k == at["affine2"]:
                                affine(n - 1, 1)
                            if k == at["gap"]:
                                gap(n - 1)
                        if first_turn:
                            for e in range(E):
                                if STEPS * d + k - 3 >= 0 and (e + 1) * NCH - 1 in chunks_at(STEPS * d + k - 3):
                                    copy_expert(e)
                if first_turn:
                    copy_expert(E - 1)

            softmax_parts()
            normalise_x(0)
            modulate(0)
            act.wait_ge(in_w_loaded, 16 * len(IN_W))
            gelu(0)
            for c in range(2):
                copy_xi(0, FWD, c)
            silu_xi(0, FWD)
            for c in range(2):
                silu_z(0, FWD, c)
            copy_xproj(0, FWD)
            for c in range(2):
                take_dt(0, FWD, c)
            use_exp_ln()
            exp_ln(0, FWD)
            rates()
            if NCH <= N_EARLY:
                copy_expert(0)
            for c in range(2):
                copy_xi(0, BWD, c)
            for i in range(COPY_AHEAD):
                copy_bc(0, FWD, i // 4, i % 4)
            if 2 * NCH <= N_EARLY:
                copy_expert(1)
            turn(0, True, False)
            with act.Fori(1, N_SEQ - 1) as n:
                turn(n, True, True)
            turn(N_SEQ - 1, False, True)
            m = N_SEQ - 1
            normalise(m, 0)
            affine(m, 0)
            normalise(m, 1)
            affine(m, 1)
            gap(m)

        @block.tensor
        def _(pe):
            pe.wait_ge(consts_ready, 1)
            pe.wait_ge(act_init, 1)
            for f in range(FB):
                last = pe.transpose(v_ps[:, 0, f * N_SEQ:(f + 1) * N_SEQ], c_sb[:, f * P:(f + 1) * P],
                                    ident[0:N_SEQ, 0:N_SEQ])
            last.then_inc(pe_init, 1)
            pe.wait_ge(dve_init, 1)
            for g in range(2):
                for f in range(FB):
                    last = pe.matmul(v_ps[0:N_SEQ, 0, g * D:(g + 1) * D], c_t[:, f, :],
                                     wmod_sb[:, f, (GA if g == 0 else GB) * D:][:, 0:D],
                                     start=(f == 0), stop=(f == FB - 1))
            for i in range(12):
                for f in range(FB):
                    last = pe.matmul(a_ps[:, 0, i * N_SEQ:(i + 1) * N_SEQ], wmod_sb[:, f, i * P:(i + 1) * P],
                                     c_t[:, f, :], start=(f == 0), stop=(f == FB - 1))
            last.then_inc(pe_init, 1)

            def mix_atoms():
                pe.wait_ge(soft_dve, 3)
                pe.transpose(v_ps[0:A, 1, 0:E], eaw_sb[:], ident[0:E, 0:E]).then_inc(soft_pe, 1)
                pe.wait_ge(soft_dve, 4)
                for c in range(NCH):
                    last = pe.matmul(v_ps[:, 1, c * E:(c + 1) * E], atoms_sb[:, c * P:(c + 1) * P], eaw_t[:],
                                     start=True, stop=True)
                last.then_inc(soft_pe, 1)

            def turn_x(m):
                pe.wait_ge(x_normed, m + 1)
                at_least(pe, a_read, 16 * m - 1)
                if isinstance(m, int) and m == 0:
                    pe.wait_ge(dve_init, 4)
                for t in range(TT):
                    for f in range(FB):
                        last = pe.transpose(a_ps[:, 0, f * T + t * P:f * T + (t + 1) * P],
                                            x_norm[:, t, f * P:(f + 1) * P], ident[:])
                last.then_inc(a_made, 1)

            def input_projection(m):
                pe.wait_ge(a_read, 16 * m + 1)
                for o in range(FB):
                    for f in range(FB):
                        last = pe.matmul(a_ps[:, 1, o * T:(o + 1) * T], w_in_sb[:, f, o * P:(o + 1) * P],
                                         h_t[:, f, :], start=(f == 0), stop=(f == FB - 1))
                last.then_inc(a_made, 1)

            def inner(m, d, which, c):
                use = (X_USE, Z_USE)[which][d] + c
                pe.wait_ge(a_read, max(a_use(0, use) - 1, IN_USE + 1) + 16 * m)
                for jj in range(2):
                    o = which * DI + (2 * c + jj) * P
                    for f in range(FB):
                        last = pe.matmul(a_ps[:, use % 2, jj * T:(jj + 1) * T], in_w_sb[:, d, f, o:o + P],
                                         h0_t[:, f, :], start=(f == 0), stop=(f == FB - 1))
                last.then_inc(a_made, 1)

            def x_projection(m, d):
                use = XP_USE[d]
                pe.wait_ge(xi_ready, 2 * m + d + 1)
                pe.wait_ge(a_read, a_use(m, use) - 1)
                for lo, hi, at in ((0, DTR, 0), (DTR, DTR + SMALL, T)):
                    for j in range(JB):
                        last = pe.matmul(a_ps[0:hi - lo, use % 2, at:at + T], xproj_sb[:, d, j, lo:hi],
                                         xi[d][:, j, :], start=(j == 0), stop=(j == JB - 1))
                last.then_inc(a_made, 1)

            def dt_projection(m, d, c):
                use = DT_USE[d] + c
                pe.wait_ge(a_read, a_use(m, XP_USE[d]) + 1 if c == 0 else a_use(m, use) - 1)
                for jj in range(2):
                    o = (2 * c + jj) * P
                    last = pe.matmul(a_ps[:, use % 2, jj * T:(jj + 1) * T], dt_w_sb[:, d, o:o + P], dtr_t[:],
                                     start=True, stop=True)
                last.then_inc(a_made, 1)

            def spread(n, d, q, r):
                un = 2 * n + d
                g = NQ * un + q
                if q == 0 and r == 0:
                    pe.wait_ge(bc_split, 2 * (un + 1))
                at_least(pe, bc_copied, 4 * g + r - 1)
                for i in range(2):
                    row = (0 if r < 2 else DS) + SQ * q + 2 * (r % 2) + i
                    last = pe.matmul(bc_ps[:, r % 2, i * T:(i + 1) * T], sel[:, row:row + 1].broadcast_to([SMALL, P]), bc[d][:],
                                     start=True, stop=True)
                last.then_inc(bc_made, 1)

            def sum_states(un, d, k):
                q, j = k // JB, k % JB
                s = STEPS * un + k
                if k in PAIRED:
                    pe.wait_ge(pairs_done, len(PAIRED) * un + PAIRED.index(k) + 1)
                else:
                    pe.wait_ge(p_done, s + 1)
                if k == 0:
                    at_least(pe, y_done, 2 * un - 1)
                if k == 2:
                    at_least(pe, y_done, 2 * un)
                if q == 0:
                    if k == 0:
                        pe.wait_ge(diag_ready, un + 1)
                    pe.matmul(y_ps[:, j, :], diag_d[:, j, :], xi[d][:, j, :], start=(j % 2 == 0), stop=False,
                              skip_group_check=True)
                parts = SQ // 2 if k in PAIRED else SQ
                for i in range(parts):
                    last = pe.matmul(y_ps[:, j, :], ident[:], h[:, k % STATE_BUFS, i, :], start=False,
                                     stop=(q == NQ - 1 and i == parts - 1), skip_group_check=True)
                last.then_inc(sum_done, 1)

            def join(m, t):
                if t == 0:
                    pe.wait_ge(out_w_loaded, 16 * (len(OUT_W) + 1))
                    pe.wait_ge(y_done, 4 * (m + 1))
                    pe.wait_ge(kept, m + 1)
                    pe.wait_ge(v_free, m + 1)
                tok = slice(t * P, (t + 1) * P)
                dst = v_ps[:, 0, t * D:(t + 1) * D]
                for d in (FWD, BWD):
                    for j in range(JB):
                        pe.matmul(dst, y_t[d][:, j, tok], out_w_sb[:, d, j, :], start=(d == 0 and j == 0),
                                  stop=False, skip_group_check=True)
                for f in range(FB):
                    last = pe.matmul(dst[:, f * P:(f + 1) * P], h0_keep[:, f, tok], ident[:], start=False, stop=True,
                                     skip_group_check=True)
                if t == TT - 1:
                    last.then_inc(r_made, 1)

            def turn_r(m, which):
                pe.wait_ge(r_normed, 2 * m + which + 1)
                for t in range(TT):
                    for f in range(FB):
                        last = pe.transpose(v_ps[:, 1, f * T + t * P:f * T + (t + 1) * P],
                                            r_norm[:, t, f * P:(f + 1) * P], ident[:])
                last.then_inc(r_turned, 1)

            def attention_out(m):
                pe.wait_ge(r_scaled, 2 * m + 1)
                for t in range(TT):
                    dst = v_ps[:, 0, t * D:(t + 1) * D]
                    for f in range(FB):
                        pe.matmul(dst, r_t[:, f, t * P:(t + 1) * P], w_out_sb[:, f, :], start=(f == 0), stop=False)
                    last = pe.matmul(dst, ones[:], b_out_sb[:], start=False, stop=True)
                last.then_inc(attn_made, 1)

            def logits(m):
                pe.wait_ge(r_scaled, 2 * m + 2)
                for t in range(TT):
                    for f in range(FB):
                        last = pe.matmul(v_ps[:, 1, t * E:(t + 1) * E], h2_t[:, f, t * P:(t + 1) * P],
                                         small[:, GW + f * E:GW + (f + 1) * E], start=(f == 0), stop=(f == FB - 1))
                last.then_inc(lg_made, 1)

            def ffn(m, c):
                t, part = c // 5, c % 5
                width = 2 * D if part < 4 else D
                if c == 1:
                    pe.wait_ge(gate_step, 12 * m + 1)
                if c >= 2:
                    pe.wait_ge(ffn_read, 10 * m + c - 1)
                for f in range(FB):
                    last = pe.matmul(v_ps[:, c % 2, 0:width], h2_t[:, f, t * P:(t + 1) * P],
                                     experts[:, f, 2 * D * part:2 * D * part + width],
                                     start=(f == 0), stop=(f == FB - 1))
                last.then_inc(ffn_made, 1)

            def expert_chunk(i):
                e, c = i // NCH, i % NCH
                pe.wait_ge(hot_made, i + 1)
                if c == 0 and e >= 2:
                    pe.wait_ge(expert_read, e - 1)
                for f in range(FB):
                    last = pe.matmul(v_ps[:, e % 2, f * D:(f + 1) * D], col_hot[:, c, f * P:(f + 1) * P],
                                     scaled_row[i % 4], start=(c == 0 and f == 0), stop=(c == NCH - 1),
                                     skip_group_check=True)
                last.then_inc(hot_used, 1)

            def turn(n, more, before):
                at = PE_AT
                first_turn = isinstance(n, int) and n == 0
                for d in (FWD, BWD):
                    unit_follows = d == FWD or more
                    for k in range(STEPS):
                        if first_turn:
                            for i in chunks_at(STEPS * d + k):
                                expert_chunk(i)
                        q, r = divmod(k + SPREAD_AHEAD, 4)
                        if q < NQ:
                            spread(n, d, q, r)
                        elif unit_follows:
                            spread(n + d, 1 - d, q - NQ, r)
                        if unit_follows:
                            m, o = n + d, 1 - d
                            if k == at["z"]:
                                inner(m, o, 1, 0)
                            if k == at["z2"]:
                                inner(m, o, 1, 1)
                            if k == at["x_proj"]:
                                x_projection(m, o)
                            if k == at["dt"]:
                                dt_projection(m, o, 0)
                            if k == at["dt2"]:
                                dt_projection(m, o, 1)
                        if d == FWD and more:
                            if k == at["turn_x"]:
                                turn_x(n + 1)
                            if k == at["w_in"]:
                                input_projection(n + 1)
                        if more and k == at["x"]:
                            inner(n + 1, d, 0, 0)
                        if more and k == at["x2"]:
                            inner(n + 1, d, 0, 1)
                        if d == FWD and before:
                            if 0 <= k - at["join"] < TT:
                                join(n - 1, k - at["join"])
                            if k == at["turn_r"]:
                                turn_r(n - 1, 0)
                            if k == at["attention"]:
                                attention_out(n - 1)
                        elif before:
                            if k == at["turn_r2"]:
                                turn_r(n - 1, 1)
                            if k == at["logits"]:
                                logits(n - 1)
                            if 0 <= k - at["ffn"] < 10:
                                ffn(n - 1, k - at["ffn"])
                        if k >= SUM_LAG:
                            sum_states(2 * n + d, d, k - SUM_LAG)
                        elif not (isinstance(n, int) and 2 * n + d == 0):
                            sum_states(2 * n + d - 1, 1 - d, k - SUM_LAG + STEPS)

            def early_chunks(group):
                for i in early(group):
                    expert_chunk(i)

            turn_x(0)
            mix_atoms()
            early_chunks(0)
            pe.wait_ge(in_w_loaded, 16 * len(IN_W))
            input_projection(0)
            early_chunks(1)
            for which in range(2):
                for c in range(2):
                    inner(0, FWD, which, c)
                early_chunks(2 + which)
            x_projection(0, FWD)
            early_chunks(4)
            for c in range(2):
                dt_projection(0, FWD, c)
            early_chunks(5)
            for c in range(2):
                inner(0, BWD, 0, c)
            for i in range(SPREAD_AHEAD):
                spread(0, FWD, i // 4, i % 4)
            early_chunks(6)
            turn(0, True, False)
            with pe.Fori(1, N_SEQ - 1) as n:
                turn(n, True, True)
            turn(N_SEQ - 1, False, True)
            for k in range(STEPS - SUM_LAG, STEPS):
                sum_states(2 * N_SEQ - 1, BWD, k)
            m = N_SEQ - 1
            join(m, 0)
            join(m, 1)
            turn_r(m, 0)
            attention_out(m)
            turn_r(m, 1)
            logits(m)
            for c in range(10):
                ffn(m, c)

        @block.vector
        def _(dve):
            def statistics(sources, st, mv, var, steps, count):
                for t in range(TT):
                    last = dve.bn_stats(st[:, t, :], sources[t])
                last.then_inc(steps, 1)
                dve.wait_ge(steps, count + 1)
                dve.memset(spare[:], 0.0)
                for t in range(TT):
                    last = dve.bn_aggr(mv[:, t, :], st[:, t, :])
                last.then_inc(steps, 1)
                dve.wait_ge(steps, count + 2)
                dve.tensor_scalar(var[:, 0, :], mv[:, :, 1], EPS, None, ALU.add)
                dve.tensor_scalar(var[:, 1, :], mv[:, :, 0], -1.0, None, ALU.mult).then_inc(steps, 1)

            def first_norm(m):
                dve.wait_ge(x_loaded, 16 * (m + 1))
                at_least(dve, x_normed, m)
                statistics([x_in[:, t, :] for t in range(TT)], x_st, x_mv, x_var, x_stats, 3 * m)

            first_norm(0)
            dve.wait_ge(pe_init, 1)
            dve.tensor_copy(c_t[:], v_ps[:, 0, 0:FB * N_SEQ].rearrange("p (f b) -> p f b", b=N_SEQ))\
                .then_inc(dve_init, 1)
            dve.wait_ge(pe_init, 2)
            raw = v_ps[0:N_SEQ, 0, 0:2 * D].rearrange("p (g f) -> p g f", f=D)
            sign = late[0:N_SEQ, 7, :].rearrange("p (g f) -> p g f", f=D)
            dve.tensor_scalar(sign, raw, 0.0, 2.0, ALU.is_ge, ALU.mult).then_inc(dve_start, 1)
            dve.tensor_scalar(mod_rows, raw, -1.0, None, ALU.mult).then_inc(dve_init, 1)
            dve.wait_ge(dve_init, 2)
            dve.tensor_tensor(mod_rows, mod_rows, raw, ALU.max).then_inc(dve_init, 1)
            dve.wait_ge(dve_start, 1)
            dve.tensor_scalar(sign, sign, 1.0, None, ALU.subtract).then_inc(dve_start, 1)
            dve.wait_ge(dve_init, 3)
            cols = a_ps[:, 0, 0:12 * N_SEQ].rearrange("p (i b) -> p b i", b=N_SEQ)
            dve.tensor_copy(mod_cols[:], cols).then_inc(dve_start, 1)
            dve.wait_ge(dve_start, 3)
            for i in (CA, CB_):
                dve.tensor_scalar(mod_cols[:, :, 2 * i:2 * i + 2], cols[:, :, 2 * i:2 * i + 2], 1.0, None, ALU.add)
            dve.scalar_tensor_tensor(out=mod_rows, in0=mod_rows, scalar=0.25, in1=sign,
                                     op0=ALU.max, op1=ALU.mult).then_inc(dve_init, 1)

            def chain(ins, count):
                ins.then_inc(dve_start, 1)
                dve.wait_ge(dve_start, count)

            def finish_norm(m, which):
                if which == 0:
                    dve.wait_ge(r_made, m + 1)
                    sources = [v_ps[:, 0, t * D:(t + 1) * D] for t in range(TT)]
                else:
                    dve.wait_ge(x1_step, 2 * (m + 1))
                    dve.wait_ge(r_normed, 2 * m + 1)
                    sources = [x1[:, t, :] for t in range(TT)]
                statistics(sources, r_st, r_mv, r_var, r_stats, 3 * (2 * m + which))

            def reset_decay(d, buf):
                first_token = 0 if d == FWD else T - 1
                dve.memset(decay[:, buf, :, first_token:first_token + 1], 0.0).then_inc(decay_reset, 1)

            def scan(n, d, k):
                un = 2 * n + d
                s = STEPS * un + k
                dve.wait_ge(exp_done, s + 1)
                dve.wait_ge(w_done, s + 1)
                if k < DECAY_BUFS:
                    dve.wait_ge(decay_reset, DECAY_BUFS * un + k + 1)
                row = scan_order(h[:, k % STATE_BUFS], d)
                dve.tensor_tensor_scan(row, scan_order(decay[:, k % DECAY_BUFS], d), row, 0.0, ALU.mult, ALU.add)\
                    .then_inc(scan_done, 1)

            def times_c(un, d, k):
                q, j = k // JB, k % JB
                if j == 0:
                    dve.wait_ge(bc_copied, 4 * (NQ * un + q) + 4)
                dve.wait_ge(scan_done, STEPS * un + k + 1)
                dve.tensor_tensor(h[:, k % STATE_BUFS], h[:, k % STATE_BUFS], c_all[:, q % 2], ALU.mult).then_inc(p_done, 1)
                if k >= STEPS - DECAY_BUFS:
                    reset_decay(1 - d, k % DECAY_BUFS)

            def conv(m, d, layer):
                un = 2 * m + d
                if layer == 0:
                    at_least(dve, sum_done, STEPS * (un - 2) + JB)
                else:
                    dve.wait_ge(conv_step, TAPS * un + layer)
                for j in range(JB):
                    at = layer if d == FWD else 2 * (TAPS - 1) - layer
                    if layer == 0 and j % 2 == 0:
                        dve.wait_ge(a_read, a_use(m, X_USE[d]) + j // 2 + 1)
                    src = x_pad[:, j, at:at + T]
                    w = col(d, CW + TAPS * j + layer)
                    if layer == 0:
                        last = dve.tensor_scalar(xi[d][:, j, :], src, w, col(d, CB + j), ALU.mult, ALU.add)
                    else:
                        last = dve.scalar_tensor_tensor(out=xi[d][:, j, :], in0=src, scalar=w,
                                                         in1=xi[d][:, j, :], op0=ALU.mult, op1=ALU.add)
                last.then_inc(conv_step, 1)

            def rounded(m, d):
                un = 2 * m + d
                dve.wait_ge(sp_made, 2 * un + 1)
                at_least(dve, w_done, STEPS * (un - 1))
                dve.tensor_scalar(u[d][:], sp_e[:], 1.0, 1.0, ALU.add, ALU.subtract).then_inc(sp_step, 1)

            def log1p(m, d):
                un = 2 * m + d
                dve.wait_ge(sp_step, SP * un + 2)
                dve.wait_ge(sp_made, 2 * un + 2)
                dve.scalar_tensor_tensor(out=u[d][:], in0=sp_l[:], scalar=-LN_MARGIN, in1=u[d][:],
                                         op0=ALU.add, op1=ALU.add).then_inc(sp_step, 1)
                dve.scalar_tensor_tensor(out=sp_e[:], in0=sp_e[:], scalar=-2.0, in1=sp_e[:],
                                         op0=ALU.add, op1=ALU.mult).then_inc(sp_step, 1)
                dve.wait_ge(sp_step, SP * un + 4)
                dve.scalar_tensor_tensor(out=u[d][:], in0=sp_e[:], scalar=-0.5, in1=u[d][:],
                                         op0=ALU.mult, op1=ALU.max).then_inc(sp_step, 1)

            def split_bc(m, d):
                un = 2 * m + d
                q1, q2 = slice(32, 64), slice(64, 96)
                dve.wait_ge(a_read, 16 * m + (7 if d == FWD else 14))
                dve.tensor_tensor(bc_rest[q2, :], bc_raw[q2, :], bc[d][q2, :], ALU.subtract)
                dve.tensor_tensor(bc_mid[q2, :], bc_raw[q2, :], bc[d][q2, :], ALU.subtract)
                dve.tensor_tensor(bc[d][q1, :], bc_raw[q1, :], bc[d][q1, :], ALU.subtract).then_inc(bc_split, 1)
                dve.wait_ge(bc_split, 2 * un + 1)
                dve.tensor_tensor(bc[d][q2, :], bc_rest[q2, :], bc_mid[q2, :], ALU.subtract).then_inc(bc_split, 1)

            def gate_y(n, d, half):
                un = 2 * n + d
                dve.wait_ge(sum_done, STEPS * un + STEPS - 2 * (1 - half))
                if half == 0:
                    at_least(dve, r_made, n)
                    if d == BWD:
                        dve.wait_ge(hot_used, NCH * E)
                part = slice(2 * half, 2 * half + 2)
                dve.tensor_tensor(y_t[d][:, part, :], y_ps[:, part, :], z[d][:, part, :], ALU.mult)\
                    .then_inc(y_done, 1)

            def residual(m):
                dve.wait_ge(attn_made, m + 1)
                dve.wait_ge(res_loaded, 48 * (m + 1))
                dve.tensor_tensor(x1, v_ps[:, 0, :].rearrange("p (t f) -> p t f", f=D),
                                  gates_bc[:, 0:1, :].broadcast_to([P, TT, D]), ALU.mult).then_inc(x1_step, 1)
                dve.wait_ge(x1_step, 2 * m + 1)
                dve.tensor_tensor(x1, x1, x_res, ALU.add).then_inc(x1_step, 1)

            def gates(m, part):
                base = 12 * m
                done = [0]

                def step(ins):
                    done[0] += 1
                    ins.then_inc(gate_step, 1)
                    dve.wait_ge(gate_step, base + done[0])

                def best(src, v, which):
                    wide = [P, TT, E]
                    step(dve.tensor_reduce(top[:, v, :], src, AX_X, ALU.max))
                    step(dve.tensor_tensor(hot[:, which], src, top[:, v, :, None].broadcast_to(wide), ALU.is_equal))
                    step(dve.tensor_tensor(hot[:, which], hot[:, which], rank[:], ALU.mult))
                    dve.tensor_reduce(top[:, 2 + v, :], hot[:, which], AX_X, ALU.max).then_inc(gate_aux, 1)
                    dve.wait_ge(gate_aux, 2 * m + which + 1)
                    return rank[:], top[:, 2 + v, :, None].broadcast_to(wide)

                if part == 0:
                    dve.wait_ge(lg_made, m + 1)
                    step(dve.tensor_scalar(lg[:], v_ps[:, 1, 0:TT * E].rearrange("p (t e) -> p t e", e=E),
                                           -50.0, 50.0, ALU.max, ALU.min))
                    a, b = best(lg[:], 0, 0)
                    dve.tensor_tensor(hot[:, 0], a, b, ALU.is_equal).then_inc(gate_aux2, 1)
                    dve.wait_ge(gate_aux2, 4 * m + 1)
                    dve.scalar_tensor_tensor(out=lg2[:], in0=hot[:, 0], scalar=-1000.0, in1=lg[:],
                                             op0=ALU.mult, op1=ALU.add).then_inc(gate_aux2, 1)
                    dve.wait_ge(gate_aux2, 4 * m + 2)
                    a, b = best(lg2[:], 1, 1)
                    dve.tensor_tensor(hot[:, 1], a, b, ALU.is_equal)
                    step(dve.tensor_tensor(soft[:, 0, :], top[:, 1, :], top[:, 0, :], ALU.subtract))
                else:
                    done[0] = 8
                    dve.wait_ge(gap_made, m + 1)
                    step(dve.tensor_scalar(soft[:, 2, :], soft[:, 1, :], 1.0, None, ALU.add))
                    step(dve.reciprocal(soft[:, 0, :], soft[:, 2, :]))
                    wide = [P, TT, E]
                    dve.tensor_tensor(soft[:, 1, :], soft[:, 1, :], soft[:, 0, :], ALU.mult)
                    step(dve.tensor_tensor(hot[:, 0], hot[:, 0], soft[:, 0, :, None].broadcast_to(wide), ALU.mult))
                    dve.tensor_tensor(hot[:, 1], hot[:, 1], soft[:, 1, :, None].broadcast_to(wide), ALU.mult)\
                        .then_inc(gate_aux2, 1)
                    dve.wait_ge(gate_aux2, 4 * m + 3)
                    dve.tensor_tensor(gate[:], hot[:, 0], hot[:, 1], ALU.add).then_inc(gate_aux2, 1)
                    dve.wait_ge(gate_aux2, 4 * m + 4)
                    step(dve.tensor_copy(soft[:, 2, :], soft[:, 0, :]))

            def weigh(m, c):
                t, part = c // 5, c % 5
                dve.wait_ge(ffn_made, 10 * m + c + 1)
                if part:
                    dve.wait_ge(ffn_read, 10 * m + c)
                if part == 4:
                    dve.tensor_tensor(acc[:, t, :], v_ps[:, c % 2, 0:D], acc[:, t, :], ALU.add).then_inc(ffn_read, 1)
                    if t == TT - 1:
                        dve.wait_ge(ffn_read, 10 * (m + 1))
                        dve.sem_inc(v_free, 1)
                    return
                e = 2 * part
                src, g = v_ps[:, c % 2, 0:D], gate[:, t, e:e + 1]
                if part == 0:
                    dve.tensor_scalar(acc[:, t, :], src, g, None, ALU.mult).then_inc(acc_step, 1)
                else:
                    dve.scalar_tensor_tensor(out=acc[:, t, :], in0=src, scalar=g, in1=acc[:, t, :],
                                             op0=ALU.mult, op1=ALU.add).then_inc(acc_step, 1)
                dve.wait_ge(acc_step, 8 * m + 4 * t + part + 1)
                dve.scalar_tensor_tensor(out=acc[:, t, :], in0=v_ps[:, c % 2, D:2 * D], scalar=gate[:, t, e + 1:e + 2],
                                         in1=acc[:, t, :], op0=ALU.mult, op1=ALU.add).then_inc(ffn_read, 1)

            def last_sums(m):
                dve.wait_ge(ffn_read, 10 * (m + 1))
                dve.tensor_tensor(acc, acc, gates_bc[:, 1:2, :].broadcast_to([P, TT, D]), ALU.mult)\
                    .then_inc(fin_step, 1)
                dve.wait_ge(fin_step, 2 * m + 1)
                dve.tensor_tensor(acc, acc, x1, ALU.add).then_inc(fin_step, 1)

            def scaled_rows(i):
                e, c = i // NCH, i % NCH
                if i >= 4:
                    dve.wait_ge(hot_used, i - 3)
                dve.tensor_scalar(scaled_row[i % 4], iota_f[:], rc_f[:, 0, c:c + 1],
                                  weighted[:, c, e:e + 1], ALU.is_equal, ALU.mult).then_inc(hot_made, 1)

            for buf in range(DECAY_BUFS):
                reset_decay(FWD, buf)
            def early_rows(group):
                for i in early(group):
                    scaled_rows(i)

            dve.wait_ge(experts_loaded, 16 * len(EXPERTS_W))
            dve.tensor_reduce(eaw_s[:, 0:1], eaw_sb[:], AX_X, ALU.max, negate=True).then_inc(soft_dve, 1)
            dve.tensor_single_scalar(rc_i[:, 0, :], idx_i[:], D.bit_length() - 1, ALU.arith_shift_right)
            chain(dve.tensor_single_scalar(rc_i[:, 1, :], idx_i[:], D - 1, ALU.bitwise_and), 4)
            dve.wait_ge(consts_ready, 1)
            dve.tensor_copy(iota_f[:], iota_i)
            chain(dve.tensor_copy(rc_f[:], rc_i[:]), 5)
            dve.wait_ge(soft_act, 1)
            dve.reciprocal(eaw_s[:, 2:3], eaw_s[:, 1:2]).then_inc(soft_dve, 1)
            dve.wait_ge(soft_dve, 2)
            dve.tensor_scalar(eaw_sb[:], eaw_sb[:], eaw_s[:, 2:3], None, ALU.mult).then_inc(soft_dve, 1)
            for c in range(NCH):
                last = dve.tensor_scalar(col_hot[:, c, :], iota_f[:], rc_f[:, 1, c:c + 1], None, ALU.is_equal)
            chain(last, 6)
            dve.wait_ge(soft_pe, 1)
            dve.tensor_copy(eaw_t[:], v_ps[0:A, 1, 0:E]).then_inc(soft_dve, 1)
            dve.wait_ge(soft_act, 2)
            chain(dve.tensor_scalar(weighted[:], weighted[:], 1.0, None, ALU.add), 7)
            chain(dve.reciprocal(weighted[:], weighted[:]), 8)
            dve.wait_ge(soft_pe, 2)
            chain(dve.tensor_tensor(weighted[:], v_ps[:, 1, 0:NCH * E].rearrange("p (c e) -> p c e", e=E),
                                    weighted[:], ALU.mult), 9)
            early_rows(0)
            early_rows(1)
            early_rows(2)
            for layer in range(TAPS):
                conv(0, FWD, layer)
            early_rows(3)
            early_rows(4)
            split_bc(0, FWD)
            early_rows(5)
            rounded(0, FWD)
            log1p(0, FWD)
            dve.wait_ge(act_init, 3)
            for d in (FWD, BWD):
                last = dve.tensor_scalar(neg_a[:, d], neg_a[:, d], -1.0, None, ALU.mult)
            last.then_inc(neg_a_ready, 1)
            early_rows(6)
            for layer in range(TAPS):
                conv(0, BWD, layer)

            def turn(n, more, before):
                at = DVE_AT
                first_turn = isinstance(n, int) and n == 0
                for d in (FWD, BWD):
                    for k in range(STEPS):
                        scan(n, d, k)
                        if k:
                            times_c(2 * n + d, d, k - 1)
                        elif not (first_turn and d == FWD):
                            times_c(2 * n + d - 1, 1 - d, STEPS - 1)
                        if first_turn:
                            for i in chunks_at(STEPS * d + k):
                                scaled_rows(i)
                        if k == at["y"] and d == FWD and not first_turn:
                            gate_y(n - 1, BWD, 1)
                        if k == at["y"] and d == BWD:
                            gate_y(n, FWD, 1)
                        if k == STEPS - 1:
                            gate_y(n, d, 0)
                        if d == FWD or more:
                            if k == at["split"]:
                                split_bc(n + d, 1 - d)
                            if k == at["rounded"]:
                                rounded(n + d, 1 - d)
                            if k == at["log1p"]:
                                log1p(n + d, 1 - d)
                        if 0 <= k - at["conv"] < TAPS and more:
                            conv(n + 1, d, k - at["conv"])
                        if d == FWD:
                            if more and k == at["stats_x"]:
                                first_norm(n + 1)
                            if before and k == at["stats_r"]:
                                finish_norm(n - 1, 0)
                            if before and k == at["residual"]:
                                residual(n - 1)
                                finish_norm(n - 1, 1)
                        elif before:
                            if k == at["gates"]:
                                gates(n - 1, 0)
                            if k == at["gates2"]:
                                gates(n - 1, 1)
                            if 0 <= k - at["weigh"] < 10:
                                weigh(n - 1, k - at["weigh"])
                            if k == STEPS - 1:
                                last_sums(n - 1)

            turn(0, True, False)
            with dve.Fori(1, N_SEQ - 1) as n:
                turn(n, True, True)
            turn(N_SEQ - 1, False, True)
            m = N_SEQ - 1
            times_c(2 * m + BWD, BWD, STEPS - 1)
            gate_y(m, BWD, 1)
            finish_norm(m, 0)
            residual(m)
            finish_norm(m, 1)
            gates(m, 0)
            gates(m, 1)
            for c in range(10):
                weigh(m, c)
            last_sums(m)


def kernel(**inputs):
    import numpy as np
    import concourse.bacc as bacc
    from concourse.bass_utils import run_bass_kernel_spmd

    a = {k[3:]: np.asarray(v) for k, v in inputs.items()}

    def blocks(w):
        return np.ascontiguousarray(w.reshape(-1, P, w.shape[-1]).transpose(1, 0, 2))

    def both(name):
        return [a[f"attn_{p}_{name}"] for p in ("fm", "bm")]

    def flat(w):
        return blocks(w).reshape(P, -1)

    packed = []
    for p in ("fm", "bm"):
        g = lambda name: a[f"attn_{p}_{name}"]
        packed += [flat(g("conv_w")), flat(g("conv_b")[:, None]), flat(g("dt_b")[:, None]), flat(g("D")[:, None]),
                   flat(g("A_log"))]
    packed += [flat(a["attn_b_in"][:, None]), flat(a["attn_ln_g"][:, None]), flat(a["attn_ln_b"][:, None]),
               flat(a["ffn_gate_w"].T)]
    xp = [np.concatenate([w[:DTR]] + [w[DTR:]] * 3).T for w in both("xproj_w")]
    arrays = {
        "x": a["attn_img_patches"],
        "smalls": np.concatenate(packed, axis=1),
        "w_in": blocks(a["attn_w_in"].T),
        "in_w": np.stack([blocks(w.T) for w in both("in_w")], axis=1),
        "xproj": np.stack([blocks(w) for w in xp], axis=1),
        "dt_w": np.stack([w.T for w in both("dt_w")], axis=1),
        "out_w": np.stack([blocks(w.T) for w in both("out_w")], axis=1),
        "w_out": blocks(a["attn_w_out"].T),
        "w_ffn": blocks(a["ffn_W"].T),
        "b_out": a["attn_b_out"][None, :],
        "eaw": a["ffn_expert_atom_weights"],
        "atoms": a["ffn_atoms"],
        "imp": blocks(a["ffn_importance"].T),
        "idx": a["ffn_mask_idx"].reshape(NCH, P).T,
        "c_in": a["c"],
        "wmod": blocks(a["wmod"]),
    }
    nc = bacc.Bacc("TRN2", target_bir_lowering=False, num_devices=1)
    fed, args = {}, []
    for name, value in arrays.items():
        value = np.ascontiguousarray(value)
        fed[f"{name}_dram"] = value
        args.append(nc.dram_tensor(f"{name}_dram", value.shape, mybir.dt.from_np(value.dtype), kind="ExternalInput").ap())
    out = nc.dram_tensor("out_dram", [N_SEQ, T, D], F32, kind="ExternalOutput").ap()
    build(nc, *args, out)
    result = run_bass_kernel_spmd(nc, [fed], core_ids=[0])
    return result.results[0]["out_dram"]
```
